# Optimizing a Trainium2 kernel written in Bass

```python
import numpy as np
import jax
import jax.numpy as jnp

def _softmax(x, axis=-1):
    return jax.nn.softmax(x, axis=axis)

def _gelu(x):
    return jax.nn.gelu(x, approximate=True)

def _silu(x):
    return jax.nn.silu(x)

def _sigmoid(x):
    return jax.nn.sigmoid(x)

def _layernorm(x, axis=-1, eps=1e-05):
    m = jnp.mean(x, axis=axis, keepdims=True)
    v = jnp.var(x, axis=axis, keepdims=True)
    return (x - m) / jnp.sqrt(v + eps)

def _scatter_add(tgt, idx, src, axis=0):
    return tgt.at[idx].add(src)

def _segment_sum(src, seg, n):
    return jax.ops.segment_sum(src, seg, n)
kernel_name = 'mk_dlrm_tower_d1_rec_r8_e80de9'

def setup_inputs(seed: int=0):
    np.random.seed(seed)
    _w = jnp.asarray

    def _rec_inputs():
        import jax
        import jax.numpy as jnp
        _tk = jax.random.key(seed)
        dense_ctx = jax.random.normal(jax.random.fold_in(_tk, 190), (1024, 16), jnp.float32)
        ids = jnp.stack([jax.random.randint(jax.random.fold_in(_tk, 200 + f), (1024,), 0, v, jnp.int32) for f, v in enumerate([125000, 125000, 1000, 1000, 1250, 125000, 12500, 1250, 1250, 1000, 12500, 1250, 1250, 1000, 1000, 1000, 1250, 12500, 1000, 1250, 12500, 1000, 12500, 1000, 1250, 1000, 1000, 12500, 1000, 1250, 1000, 1000])], axis=1)
        tbl_0 = 0.05 * jax.random.normal(jax.random.fold_in(_tk, 500 + 0), (125000, 64), jnp.float32)
        tbl_1 = 0.05 * jax.random.normal(jax.random.fold_in(_tk, 500 + 1), (125000, 64), jnp.float32)
        tbl_2 = 0.05 * jax.random.normal(jax.random.fold_in(_tk, 500 + 2), (1000, 64), jnp.float32)
        tbl_3 = 0.05 * jax.random.normal(jax.random.fold_in(_tk, 500 + 3), (1000, 64), jnp.float32)
        tbl_4 = 0.05 * jax.random.normal(jax.random.fold_in(_tk, 500 + 4), (1250, 64), jnp.float32)
        tbl_5 = 0.05 * jax.random.normal(jax.random.fold_in(_tk, 500 + 5), (125000, 64), jnp.float32)
        tbl_6 = 0.05 * jax.random.normal(jax.random.fold_in(_tk, 500 + 6), (12500, 64), jnp.float32)
        tbl_7 = 0.05 * jax.random.normal(jax.random.fold_in(_tk, 500 + 7), (1250, 64), jnp.float32)
        tbl_8 = 0.05 * jax.random.normal(jax.random.fold_in(_tk, 500 + 8), (1250, 64), jnp.float32)
        tbl_9 = 0.05 * jax.random.normal(jax.random.fold_in(_tk, 500 + 9), (1000, 64), jnp.float32)
        tbl_10 = 0.05 * jax.random.normal(jax.random.fold_in(_tk, 500 + 10), (12500, 64), jnp.float32)
        tbl_11 = 0.05 * jax.random.normal(jax.random.fold_in(_tk, 500 + 11), (1250, 64), jnp.float32)
        tbl_12 = 0.05 * jax.random.normal(jax.random.fold_in(_tk, 500 + 12), (1250, 64), jnp.float32)
        tbl_13 = 0.05 * jax.random.normal(jax.random.fold_in(_tk, 500 + 13), (1000, 64), jnp.float32)
        tbl_14 = 0.05 * jax.random.normal(jax.random.fold_in(_tk, 500 + 14), (1000, 64), jnp.float32)
        tbl_15 = 0.05 * jax.random.normal(jax.random.fold_in(_tk, 500 + 15), (1000, 64), jnp.float32)
        tbl_16 = 0.05 * jax.random.normal(jax.random.fold_in(_tk, 500 + 16), (1250, 64), jnp.float32)
        tbl_17 = 0.05 * jax.random.normal(jax.random.fold_in(_tk, 500 + 17), (12500, 64), jnp.float32)
        tbl_18 = 0.05 * jax.random.normal(jax.random.fold_in(_tk, 500 + 18), (1000, 64), jnp.float32)
        tbl_19 = 0.05 * jax.random.normal(jax.random.fold_in(_tk, 500 + 19), (1250, 64), jnp.float32)
        tbl_20 = 0.05 * jax.random.normal(jax.random.fold_in(_tk, 500 + 20), (12500, 64), jnp.float32)
        tbl_21 = 0.05 * jax.random.normal(jax.random.fold_in(_tk, 500 + 21), (1000, 64), jnp.float32)
        tbl_22 = 0.05 * jax.random.normal(jax.random.fold_in(_tk, 500 + 22), (12500, 64), jnp.float32)
        tbl_23 = 0.05 * jax.random.normal(jax.random.fold_in(_tk, 500 + 23), (1000, 64), jnp.float32)
        tbl_24 = 0.05 * jax.random.normal(jax.random.fold_in(_tk, 500 + 24), (1250, 64), jnp.float32)
        tbl_25 = 0.05 * jax.random.normal(jax.random.fold_in(_tk, 500 + 25), (1000, 64), jnp.float32)
        tbl_26 = 0.05 * jax.random.normal(jax.random.fold_in(_tk, 500 + 26), (1000, 64), jnp.float32)
        tbl_27 = 0.05 * jax.random.normal(jax.random.fold_in(_tk, 500 + 27), (12500, 64), jnp.float32)
        tbl_28 = 0.05 * jax.random.normal(jax.random.fold_in(_tk, 500 + 28), (1000, 64), jnp.float32)
        tbl_29 = 0.05 * jax.random.normal(jax.random.fold_in(_tk, 500 + 29), (1250, 64), jnp.float32)
        tbl_30 = 0.05 * jax.random.normal(jax.random.fold_in(_tk, 500 + 30), (1000, 64), jnp.float32)
        tbl_31 = 0.05 * jax.random.normal(jax.random.fold_in(_tk, 500 + 31), (1000, 64), jnp.float32)
        _rk = jax.random.fold_in(_tk, 7)
        W_top1 = 0.0428746 * jax.random.normal(jax.random.fold_in(_tk, 801), (544, 512), jnp.float32)
        W_top2 = 0.0441942 * jax.random.normal(jax.random.fold_in(_tk, 802), (512, 256), jnp.float32)
        W_top3 = 0.0625 * jax.random.normal(jax.random.fold_in(_tk, 803), (256, 1), jnp.float32)
        b_top1 = jnp.zeros((512,), jnp.float32)
        b_top2 = jnp.zeros((256,), jnp.float32)
        return (dense_ctx, ids, tbl_0, tbl_1, tbl_2, tbl_3, tbl_4, tbl_5, tbl_6, tbl_7, tbl_8, tbl_9, tbl_10, tbl_11, tbl_12, tbl_13, tbl_14, tbl_15, tbl_16, tbl_17, tbl_18, tbl_19, tbl_20, tbl_21, tbl_22, tbl_23, tbl_24, tbl_25, tbl_26, tbl_27, tbl_28, tbl_29, tbl_30, tbl_31, W_top1, b_top1, W_top2, b_top2, W_top3)
    dense_ctx, ids, tbl_0, tbl_1, tbl_2, tbl_3, tbl_4, tbl_5, tbl_6, tbl_7, tbl_8, tbl_9, tbl_10, tbl_11, tbl_12, tbl_13, tbl_14, tbl_15, tbl_16, tbl_17, tbl_18, tbl_19, tbl_20, tbl_21, tbl_22, tbl_23, tbl_24, tbl_25, tbl_26, tbl_27, tbl_28, tbl_29, tbl_30, tbl_31, W_top1, b_top1, W_top2, b_top2, W_top3 = _rec_inputs()

    def _L0_rec_setup():
        import jax, jax.numpy as jnp
        import numpy as np
        B, F, D = (512, 32, 64)
        II, JJ = np.triu_indices(F, k=1)
        P = II.shape[0]
        key = jax.random.key(seed)
        kx, kk = jax.random.split(key)
        x = jax.random.normal(kx, (B, F, D), dtype=jnp.float32)
        kernels = jax.random.normal(kk, (P, D, D), dtype=jnp.float32) * 0.001
        return {'x': x, 'kernels': kernels}
    _L0_rec_all = _L0_rec_setup()
    _L0_rec_in = {k: v for k, v in _L0_rec_all.items() if k in ('kernels',)}
    del _L0_rec_all
    return {'dense_ctx': dense_ctx, 'ids': ids, 'tbl_0': tbl_0, 'tbl_1': tbl_1, 'tbl_2': tbl_2, 'tbl_3': tbl_3, 'tbl_4': tbl_4, 'tbl_5': tbl_5, 'tbl_6': tbl_6, 'tbl_7': tbl_7, 'tbl_8': tbl_8, 'tbl_9': tbl_9, 'tbl_10': tbl_10, 'tbl_11': tbl_11, 'tbl_12': tbl_12, 'tbl_13': tbl_13, 'tbl_14': tbl_14, 'tbl_15': tbl_15, 'tbl_16': tbl_16, 'tbl_17': tbl_17, 'tbl_18': tbl_18, 'tbl_19': tbl_19, 'tbl_20': tbl_20, 'tbl_21': tbl_21, 'tbl_22': tbl_22, 'tbl_23': tbl_23, 'tbl_24': tbl_24, 'tbl_25': tbl_25, 'tbl_26': tbl_26, 'tbl_27': tbl_27, 'tbl_28': tbl_28, 'tbl_29': tbl_29, 'tbl_30': tbl_30, 'tbl_31': tbl_31, 'W_top1': W_top1, 'b_top1': b_top1, 'W_top2': W_top2, 'b_top2': b_top2, 'W_top3': W_top3, 'L0_rec_kernels': _L0_rec_in['kernels']}

def reference(dense_ctx, ids, tbl_0, tbl_1, tbl_2, tbl_3, tbl_4, tbl_5, tbl_6, tbl_7, tbl_8, tbl_9, tbl_10, tbl_11, tbl_12, tbl_13, tbl_14, tbl_15, tbl_16, tbl_17, tbl_18, tbl_19, tbl_20, tbl_21, tbl_22, tbl_23, tbl_24, tbl_25, tbl_26, tbl_27, tbl_28, tbl_29, tbl_30, tbl_31, W_top1, b_top1, W_top2, b_top2, W_top3, L0_rec_kernels):
    import jax
    import jax.numpy as jnp

    def _L0_rec_ref(x, kernels):
        import jax, jax.numpy as jnp
        import numpy as np
        B, F, D = (512, 32, 64)
        II, JJ = np.triu_indices(F, k=1)
        P = II.shape[0]
        z = jnp.sum(x, axis=-1)
        xi = x[:, II, :]
        xj = x[:, JJ, :]
        outer = jnp.einsum('bpd,pde,bpe->bp', xi, kernels, xj)
        return jnp.concatenate([z, outer], axis=1)
    e = jnp.stack([tbl_0[ids[:, 0]], tbl_1[ids[:, 1]], tbl_2[ids[:, 2]], tbl_3[ids[:, 3]], tbl_4[ids[:, 4]], tbl_5[ids[:, 5]], tbl_6[ids[:, 6]], tbl_7[ids[:, 7]], tbl_8[ids[:, 8]], tbl_9[ids[:, 9]], tbl_10[ids[:, 10]], tbl_11[ids[:, 11]], tbl_12[ids[:, 12]], tbl_13[ids[:, 13]], tbl_14[ids[:, 14]], tbl_15[ids[:, 15]], tbl_16[ids[:, 16]], tbl_17[ids[:, 17]], tbl_18[ids[:, 18]], tbl_19[ids[:, 19]], tbl_20[ids[:, 20]], tbl_21[ids[:, 21]], tbl_22[ids[:, 22]], tbl_23[ids[:, 23]], tbl_24[ids[:, 24]], tbl_25[ids[:, 25]], tbl_26[ids[:, 26]], tbl_27[ids[:, 27]], tbl_28[ids[:, 28]], tbl_29[ids[:, 29]], tbl_30[ids[:, 30]], tbl_31[ids[:, 31]]], axis=1)
    z = _L0_rec_ref(e, L0_rec_kernels)
    z = z.reshape(z.shape[0], -1)
    h = jnp.concatenate([z, dense_ctx], axis=1)
    h = jnp.maximum(h @ W_top1 + b_top1, 0.0)
    h = jnp.maximum(h @ W_top2 + b_top2, 0.0)
    y = h @ W_top3
    return y

_drawn_inputs = setup_inputs


def setup_inputs(seed=0):
    import zlib

    import numpy as np

    out = dict(_drawn_inputs(seed))
    spreads = {'b_top1': (0.0, 0.1), 'b_top2': (0.0, 0.1)}
    factors = {'L0_rec_kernels': 64.0}
    for name, (base, spread) in spreads.items():
        noise = np.random.default_rng([zlib.crc32(name.encode()), seed]).standard_normal(out[name].shape)
        drawn = base * np.exp(spread * noise) if base else spread * noise
        out[name] = jnp.asarray(drawn.astype(out[name].dtype))
    for name, factor in factors.items():
        out[name] = (out[name] * factor).astype(out[name].dtype)
    return out
```

```python
import concourse.bass as bass
from concourse import mybir
from contextlib import ExitStack

PART = 128
B = 1024
F = 32
D = 64
NF = F // 2
DENSE = 16
H1, H2 = 512, 256
HB = 512
HALVES = B // HB
BT = HB // PART
GROUP = 4
ROWS = 32
PER_Z = GROUP * (ROWS // 2)
DENSE_ROW = 8


def tile_order():
    order = []
    for i in range(F - 2, -1, -1):
        ms = list(range((i + 1) // 2, NF))
        order += [(i, m) for m in (ms if i % 2 else ms[::-1])]
    return order


TILES = tile_order()
UNITS = len(TILES) // 2
for _u in range(UNITS):
    if TILES[2 * _u][1] > TILES[2 * _u + 1][1]:
        TILES[2 * _u], TILES[2 * _u + 1] = TILES[2 * _u + 1], TILES[2 * _u]
Z_TILES = len(TILES) // PER_Z + 1
K_COLS = len(TILES) * PART
K_CHUNK = 1024
K_CHUNKS = K_COLS // K_CHUNK
TILES_A_CHUNK = K_CHUNK // PART


def z_row(t):
    g = t // GROUP
    return t // PER_Z, ROWS * (t % GROUP) + 2 * (g % (ROWS // 2))


def build(nc, ids, tables, kmat, dense_t, w1, b1, w2, b2, w3, out):
    fp32, fp32r, i32 = mybir.dt.float32, mybir.dt.float32r, mybir.dt.int32
    ALU, ACT = mybir.AluOpType, mybir.ActivationFunctionType

    T_SLOTS = 3
    P_SLOTS = 4
    X_SLOTS = 8
    XA_SLOTS = 2
    PAIR_ROWS = 2 * D
    N1, N2 = H1 // PART, H2 // PART

    z_dram = nc.dram_tensor("z_scratch", (Z_TILES, PART, B), fp32, kind="Internal").ap()

    with ExitStack() as ctx:
        def sb(name, shape, dt=fp32):
            return ctx.enter_context(nc.sbuf_tensor(name, shape, dt))

        def sem(name):
            return ctx.enter_context(nc.semaphore(name))

        k_split = sb("k_split", [PART, K_COLS], fp32r)
        x2 = sb("x2", [PART, NF, HB])
        prod = sb("prod", [PART, P_SLOTS, 2 * HB])
        x_high = sb("x_high", [PART, XA_SLOTS, HB], fp32r)
        x_low = sb("x_low", [PART, XA_SLOTS, HB], fp32r)
        x_nat = sb("x_nat", [PART, X_SLOTS, BT, PAIR_ROWS])
        x_dup = sb("x_dup", [PART, BT, 2, D])
        z_out = sb("z_out", [PART, HB])
        ids_all = sb("ids_all", [PART, HALVES * BT * F], i32)
        ids_now = sb("ids_now", [PART, BT * F], i32)
        ident = sb("ident", [PART, PART])
        SEL0 = ROWS - 2
        select = sb("select", [PART, SEL0 + ROWS])
        b1_sb = sb("b1_sb", [PART, N1])
        b2_sb = sb("b2_sb", [PART, N2])
        w3_sb = sb("w3_sb", [PART, N2])

        t_ps = ctx.enter_context(nc.psum_tensor("t_ps", [PART, T_SLOTS, 2 * HB], fp32))
        z_ps = ctx.enter_context(nc.psum_tensor("z_ps", [PART, HB], fp32))
        xt_ps = ctx.enter_context(nc.psum_tensor("xt_ps", [PART, HB], fp32))

        w_flat = x_nat[:, :, :, :].rearrange("p s b c -> p (s b c)")
        w1_sb = w_flat[:, 0:Z_TILES * H1].rearrange("p (k n) -> p k n", n=H1)
        w2_sb = w_flat[:, Z_TILES * H1:Z_TILES * H1 + N1 * H2].rearrange("p (k n) -> p k n", n=H2)
        x2_flat = x2[:, :, :].rearrange("p m b -> p (m b)")
        z_sb = x2_flat[:, 0:Z_TILES * B].rearrange("p (k b) -> p k b", b=B)
        p_flat = prod[:, :, :].rearrange("p s b -> p (s b)")
        x2_left = x2_flat[:, Z_TILES * B:]
        h1_sb = [f[:, 0:N1 * HB].rearrange("p (n b) -> p n b", b=HB) for f in (p_flat, x2_left)]
        y_sb = p_flat[0:1, (N1 + N2) * HB:(N1 + N2) * HB + B]
        h2_sb = [f[:, N1 * HB:(N1 + N2) * HB].rearrange("p (n b) -> p n b", b=HB) for f in (p_flat, x2_left)]

        s_small = sem("small_loaded")
        s_kraw = [sem(f"k_raw_loaded{n}") for n in range(P_SLOTS)]
        s_khigh = sem("k_high_ready")
        s_klow = sem("k_low_ready")
        s_const = sem("constants_ready")
        s_ids = sem("ids_now_ready")
        s_pairs = sem("pool_went_on")
        s_gather = [[sem(f"gathered{n}_{r}") for r in range(2)] for n in range(X_SLOTS)]
        s_dup = sem("x_dup_ready")
        s_xt = sem("x_transposed")
        s_x2 = sem("x2_ready")
        s_xlow = sem("x_low_ready")
        s_main = sem("t_ready")
        s_prod = sem("prod_ready")
        s_sum = sem("sums_done")
        s_xsum = sem("x_sums_done")
        s_zout = sem("z_out_ready")
        s_zstore = sem("z_stored")
        s_zfree = sem("z_out_free")
        s_weights = sem("weights_loaded")
        s_zload = sem("z_loaded")
        s_layer = sem("layer_outputs_in_psum")
        s_act = sem("layer_outputs_in_sbuf")
        s_out = sem("out_stored")

        DUP_CREDIT = 2 * X_SLOTS
        XT_CREDIT = 1
        PROD_CREDIT = T_SLOTS
        SUM_CREDIT = P_SLOTS // 2
        XSUM_CREDIT = 1
        ZOUT_CREDIT = 2
        ZFREE_CREDIT = 1

        SUMS = len(TILES) // GROUP
        SUMS_A_Z = PER_Z // GROUP
        SPLITS = F - 1
        LAST_Z = Z_TILES - 1
        units_until = {i: max(n for n, (j, _) in enumerate(TILES) if j == i) // 2 + 1 for i in range(F - 1)}
        first_unit = {i: min(n for n, (j, _) in enumerate(TILES) if j == i) // 2 for i in range(F - 1)}

        plan = []
        prepped, summed = F, 0
        for u in range(UNITS):
            i_now = min(TILES[2 * u][0], TILES[2 * u + 1][0])
            own = [n for n, (i, _) in enumerate(TILES) if i == i_now]
            while prepped > i_now:
                prepped -= 1
                plan.append(("feature", prepped))
            plan.append(("unit", u))
            if i_now > 0 and prepped == i_now and 2 * u + 1 >= own[len(own) // 2]:
                prepped -= 1
                plan.append(("feature", prepped))
            if u % 2 == 0 and u >= 2:
                plan.append(("sum", summed))
                summed += 1
            if u == UNITS - 5:
                plan.append(("embedding sums", 0))
        while summed < SUMS:
            plan.append(("sum", summed))
            summed += 1
        z_order = []
        for what, n in plan:
            if what == "sum" and n % SUMS_A_Z == SUMS_A_Z - 1:
                z_order.append(n // SUMS_A_Z)
            elif what == "embedding sums":
                z_order.append(LAST_Z)

        LAYERS = [(1, hb, n) for hb in range(HALVES) for n in range(N1)]
        LAYERS += [(2, hb, n) for hb in range(HALVES) for n in range(N2)]
        LAYERS += [(3, hb, 0) for hb in range(HALVES)]
        BANKS = 2 * T_SLOTS

        def bank(q):
            return t_ps[:, q % BANKS // 2, q % 2 * HB:q % 2 * HB + HB]

        block = ctx.enter_context(nc.Block())

        @block.sync
        def _(sp):
            sp.dma_start(ids_all[:, :], ids).then_inc(s_small, 16)
            for slot in range(P_SLOTS):
                for half in range(2):
                    sp.dma_start(prod[D * half:D * half + D, slot, :], kmat[slot]).then_inc(s_kraw[slot], 16)
            sp.dma_start(b1_sb[:, :], b1).then_inc(s_small, 16)
            sp.dma_start(b2_sb[:, :], b2).then_inc(s_small, 16)
            sp.dma_start(w3_sb[:, :], w3).then_inc(s_small, 16)
            with sp.Fori(1, K_CHUNKS // P_SLOTS) as r:
                for slot in range(P_SLOTS):
                    sp.wait_ge(s_klow, r * P_SLOTS + (slot + 1 - P_SLOTS))
                    src = kmat[bass.ds(r * P_SLOTS + slot, 1)].rearrange("c p n -> (c p) n")
                    for half in range(2):
                        sp.dma_start(prod[D * half:D * half + D, slot, :], src).then_inc(s_kraw[slot], 16)
            with sp.Fori(0, HALVES) as h:
                for n, zt in enumerate(z_order):
                    sp.wait_ge(s_zout, h * Z_TILES + (n + 1 + ZOUT_CREDIT))
                    sp.dma_start(z_dram[zt][:, bass.ds(h * HB, HB)], z_out[:, :]).then_inc(s_zstore, 16)
                    sp.wait_ge(s_zstore, h * (16 * Z_TILES) + 16 * (n + 1))
                    sp.sem_inc(s_zfree, 1)
            sp.wait_ge(s_dup, HALVES * F + DUP_CREDIT)
            sp.dma_start(w1_sb, w1).then_inc(s_weights, 16)
            sp.dma_start(w2_sb, w2).then_inc(s_weights, 16)
            sp.wait_ge(s_prod, HALVES * UNITS + PROD_CREDIT)
            sp.wait_ge(s_xsum, HALVES + XSUM_CREDIT)
            for zt in range(LAST_Z):
                sp.dma_start(z_sb[:, zt, :], z_dram[zt]).then_inc(s_zload, 16)
            lo, hi = DENSE_ROW, DENSE_ROW + DENSE
            sp.dma_start(z_sb[0:lo, LAST_Z, :], z_dram[LAST_Z][0:lo, :]).then_inc(s_zload, 16)
            sp.dma_start(z_sb[lo:hi, LAST_Z, :], dense_t).then_inc(s_zload, 16)
            sp.dma_start(z_sb[hi:PART, LAST_Z, :], z_dram[LAST_Z][hi:PART, :]).then_inc(s_zload, 16)
            sp.wait_ge(s_act, len(LAYERS))
            sp.dma_start(out, y_sb[:, :]).then_inc(s_out, 16)
            sp.wait_ge(s_out, 16)

        @block.gpsimd
        def _(pool):
            nc.gpsimd.memset(ident[:, :], 0.0).then_inc(s_const, 1)
            nc.gpsimd.memset(select[:, :], 0.0).then_inc(s_const, 1)
            pool.wait_ge(s_small, 64)
            nc.gpsimd.tensor_copy(ids_now[:, :], ids_all[:, 0:BT * F]).then_inc(s_ids, 1)
            pool.wait_ge(s_const, 2)
            nc.gpsimd.affine_select(out=ident[:, :], in_=ident[:, :], compare_op=ALU.not_equal, fill=1.0,
                                    base=0, pattern=[[-1, PART]], channel_multiplier=1).then_inc(s_const, 1)
            pool.wait_ge(s_const, 3)
            nc.gpsimd.memset(select[0:D, SEL0:SEL0 + 1], 1.0).then_inc(s_const, 1)
            pool.wait_ge(s_const, 4)
            nc.gpsimd.memset(select[D:PART, SEL0 + 1:SEL0 + 2], 1.0).then_inc(s_const, 1)
            pool.sem_inc(s_dup, DUP_CREDIT)
            pool.sem_inc(s_xt, XT_CREDIT)
            pool.sem_inc(s_prod, PROD_CREDIT)
            pool.sem_inc(s_sum, SUM_CREDIT)
            pool.sem_inc(s_xsum, XSUM_CREDIT)
            pool.sem_inc(s_zout, ZOUT_CREDIT)
            pool.sem_inc(s_zfree, ZFREE_CREDIT)
            with pool.Fori(0, HALVES) as h:
                pool.wait_ge(s_ids, h + 1)
                pool.sem_inc(s_pairs, 1)
                for n in range(NF):
                    m, slot = NF - 1 - n, n % X_SLOTS
                    pool.wait_ge(s_dup, h * F + 2 * (n + 1))
                    pool.sem_inc(s_pairs, 1)
                    for r in (1, 0):
                        f = 2 * m + r
                        for bt in range(BT):
                            nc.gpsimd.indirect_dma_start(
                                x_nat[:, slot, bt, D * r:D * r + D], None, tables[f],
                                bass.IndirectOffsetOnAxis(ap=ids_now[:, bt * F + f:bt * F + f + 1], axis=0),
                            ).then_inc(s_gather[slot][r], 16)
                for slot in range(X_SLOTS):
                    for r in range(2):
                        pool.wait_ge(s_gather[slot][r], (h + 1) * (16 * BT * NF // X_SLOTS))
                        pool.sem_inc(s_pairs, 1)
                nc.gpsimd.tensor_copy(ids_now[:, :], ids_all[:, bass.ds((HALVES - 1 - h) * (BT * F), BT * F)])\
                    .then_inc(s_ids, 1)

        @block.scalar
        def _(act):
            with act.Fori(0, K_CHUNKS // P_SLOTS) as r:
                for slot in range(P_SLOTS):
                    act.wait_ge(s_kraw[slot], (r + 1) * 32)
                    nc.scalar.activation(k_split[:, bass.ds((r * P_SLOTS + slot) * K_CHUNK, K_CHUNK)],
                                         prod[:, slot, :], ACT.Copy).then_inc(s_khigh, 1)

            with act.Fori(0, HALVES) as h:
                def feature(i):
                    m, slot = i // 2, (NF - 1 - i // 2) % X_SLOTS
                    act.wait_ge(s_gather[slot][i % 2],
                                h * (16 * BT * NF // X_SLOTS) + 16 * BT * ((NF - 1 - m) // X_SLOTS + 1))
                    act.wait_ge(s_xt, h * F + (F - 1 - i + XT_CREDIT))
                    rows = x_nat[:, slot, :, D * (i % 2):D * (i % 2) + D]
                    nc.scalar.activation(x_dup[:, :, :, :], rows.unsqueeze(2).broadcast_to([PART, BT, 2, D]),
                                         ACT.Copy).then_inc(s_dup, 1)
                    if i < F - 1:
                        if i + 2 < F - 1:
                            act.wait_ge(s_main, h * UNITS + units_until[i + 2])
                        act.wait_ge(s_xt, h * F + (F - i + XT_CREDIT))
                        nc.scalar.activation(x_high[:, i % XA_SLOTS, :], xt_ps[:, :], ACT.Copy)
                    else:
                        act.wait_ge(s_prod, h * UNITS + PROD_CREDIT)
                        act.wait_ge(s_xsum, h + XSUM_CREDIT)
                        act.wait_ge(s_xt, h * F + (F - i + XT_CREDIT))
                    rows = slice(D * (i % 2), D * (i % 2) + D)
                    nc.scalar.activation(x2[rows, i // 2, :], xt_ps[rows, :], ACT.Copy).then_inc(s_x2, 1)

                def z_tile(n, src):
                    act.wait_ge(s_zfree, h * Z_TILES + (n + ZFREE_CREDIT))
                    nc.scalar.activation(z_out[:, :], src[:, :], ACT.Copy).then_inc(s_zout, 1)

                n = 0
                for what, k in plan:
                    if what == "feature":
                        feature(k)
                    elif what == "sum" and k % SUMS_A_Z == SUMS_A_Z - 1:
                        act.wait_ge(s_sum, h * SUMS + (k + 1 + SUM_CREDIT))
                        z_tile(n, z_ps)
                        n += 1
                    elif what == "embedding sums":
                        act.wait_ge(s_xsum, h + (1 + XSUM_CREDIT))
                        z_tile(n, xt_ps)
                        n += 1

            act.wait_ge(s_small, 64)
            for q, (layer, hb, n) in enumerate(LAYERS):
                act.wait_ge(s_layer, q + 1)
                if layer == 1:
                    nc.scalar.activation(h1_sb[hb][:, n, :], bank(q), ACT.Relu, bias=b1_sb[:, n:n + 1]).then_inc(s_act, 1)
                elif layer == 2:
                    nc.scalar.activation(h2_sb[hb][:, n, :], bank(q), ACT.Relu, bias=b2_sb[:, n:n + 1]).then_inc(s_act, 1)
                else:
                    nc.scalar.activation(y_sb[0:1, hb * HB:hb * HB + HB], bank(q)[0:1, :], ACT.Copy).then_inc(s_act, 1)

        @block.vector
        def _(dve):
            with dve.Fori(0, K_CHUNKS // P_SLOTS) as r:
                for slot in range(P_SLOTS):
                    dve.wait_ge(s_khigh, r * P_SLOTS + (slot + 1))
                    low = k_split[D:PART, bass.ds((r * P_SLOTS + slot) * K_CHUNK, K_CHUNK)]
                    nc.vector.tensor_tensor(low, prod[D:PART, slot, :], low.bitcast(fp32), ALU.subtract).then_inc(s_klow, 1)

            with dve.Fori(0, HALVES) as h:
                waiting = []

                def low_part():
                    i = waiting.pop(0)
                    dve.wait_ge(s_x2, h * F + (F - i))
                    nc.vector.tensor_tensor(x_low[:, i % XA_SLOTS, :], xt_ps[:, :],
                                            x_high[:, i % XA_SLOTS, :].bitcast(fp32), ALU.subtract).then_inc(s_xlow, 1)

                for what, k in plan:
                    if what == "feature" and k < F - 1:
                        if waiting:
                            low_part()
                        waiting.append(k)
                    if what != "unit":
                        continue
                    (ia, ma), (ib, mb) = TILES[2 * k], TILES[2 * k + 1]
                    if waiting and waiting[0] >= min(ia, ib):
                        low_part()
                    dve.wait_ge(s_main, h * UNITS + (k + 1))
                    if k == first_unit[min(ia, ib)]:
                        dve.wait_ge(s_x2, h * F + (F - min(ia, ib)))
                    if k % 2 == 0:
                        dve.wait_ge(s_sum, h * SUMS + (k // 2 + 1))
                    if ma == mb:
                        xj = x2[:, ma:ma + 1, :].broadcast_to([PART, 2, HB])
                    else:
                        xj = x2[:, ma:mb + 1, :]
                    view = lambda t: t.rearrange("p (t b) -> p t b", b=HB)
                    nc.vector.tensor_tensor(view(prod[:, k % P_SLOTS, :]), view(t_ps[:, k % T_SLOTS, :]), xj,
                                            ALU.mult).then_inc(s_prod, 1)
                    if waiting:
                        low_part()

        @block.tensor
        def _(pe):
            pe.wait_ge(s_const, 5)
            with pe.Fori(0, HALVES) as h:
                def feature(i):
                    pe.wait_ge(s_dup, h * F + (F - i + DUP_CREDIT))
                    if i == F - 1:
                        pe.wait_ge(s_zout, h * Z_TILES + 1)
                    else:
                        pe.wait_ge(s_x2, h * F + (F - 1 - i))
                        if i < F - 2:
                            pe.wait_ge(s_xlow, h * SPLITS + (F - 2 - i))
                    for bt in range(BT):
                        last = nc.tensor.transpose(xt_ps[:, bt * PART:bt * PART + PART],
                                                   x_dup[:, bt, :, :].rearrange("p r d -> p (r d)"), ident[:, :])
                    last.then_inc(s_xt, 1)

                def unit(u):
                    pe.wait_ge(s_prod, h * UNITS + max(u + 1, PROD_CREDIT))
                    for t in (2 * u, 2 * u + 1):
                        i, m = TILES[t]
                        if u == first_unit[i]:
                            pe.wait_ge(s_xlow, h * SPLITS + (F - 1 - i))
                        if t % TILES_A_CHUNK == 0:
                            pe.wait_ge(s_klow, t // TILES_A_CHUNK + 1)
                        dst = t_ps[:, u % T_SLOTS, t % 2 * HB:t % 2 * HB + HB]
                        weights = k_split[:, t * PART:t * PART + PART]
                        nc.tensor.matmul(dst, weights, x_high[:, i % XA_SLOTS, :], start=True, stop=False)
                        last = nc.tensor.matmul(dst, weights, x_low[:, i % XA_SLOTS, :], start=False, stop=True)
                    last.then_inc(s_main, 1)

                def selector(k):
                    return select[:, SEL0 - 2 * k:SEL0 - 2 * k + ROWS]

                def sum_round(g):
                    pe.wait_ge(s_prod, h * UNITS + (2 * g + 2 + PROD_CREDIT))
                    k = g % SUMS_A_Z
                    if g == 0:
                        pe.wait_ge(s_zout, h * Z_TILES + ZOUT_CREDIT)
                    elif k == 0:
                        pe.wait_ge(s_zout, h * Z_TILES + (z_order.index(g // SUMS_A_Z - 1) + 1 + ZOUT_CREDIT))
                    for c in range(GROUP):
                        u = 2 * g + c // 2
                        last = nc.tensor.matmul(z_ps[ROWS * c:ROWS * c + ROWS, :], selector(k),
                                                prod[:, u % P_SLOTS, c % 2 * HB:c % 2 * HB + HB],
                                                start=(k == 0), stop=(k == SUMS_A_Z - 1))
                    last.then_inc(s_sum, 1)

                def embedding_sums():
                    pe.wait_ge(s_x2, h * F + F)
                    pe.wait_ge(s_xlow, h * SPLITS + SPLITS)
                    for m in range(NF):
                        k, c = m // GROUP, m % GROUP
                        last = nc.tensor.matmul(xt_ps[ROWS * c:ROWS * c + ROWS, :], selector(k), x2[:, m, :],
                                                start=(k == 0), stop=(k == NF // GROUP - 1))
                    last.then_inc(s_xsum, 1)

                steps = {"feature": feature, "unit": unit, "sum": sum_round, "embedding sums": lambda _: embedding_sums()}
                for what, k in plan:
                    steps[what](k)

            pe.wait_ge(s_weights, 32)
            pe.wait_ge(s_zload, 16 * (Z_TILES + 2))
            pe.wait_ge(s_prod, HALVES * UNITS + PROD_CREDIT)
            need = {2: N1, 3: N2}
            for q, (layer, hb, n) in enumerate(LAYERS):
                ready = q - BANKS + 1
                if layer > 1:
                    ready = max(ready, 1 + max(p for p, (la, b, _) in enumerate(LAYERS) if (la, b) == (layer - 1, hb)))
                if ready > 0:
                    pe.wait_ge(s_act, ready)
                lots, rows = {1: (Z_TILES, PART), 2: (N1, PART), 3: (N2, 1)}[layer]
                for k in range(lots):
                    if layer == 1:
                        w, x = w1_sb[:, k, n * PART:n * PART + PART], z_sb[:, k, hb * HB:hb * HB + HB]
                    elif layer == 2:
                        w, x = w2_sb[:, k, n * PART:n * PART + PART], h1_sb[hb][:, k, :]
                    else:
                        w, x = w3_sb[:, k:k + 1], h2_sb[hb][:, k, :]
                    last = nc.tensor.matmul(bank(q)[0:rows, :], w, x, start=(k == 0), stop=(k == lots - 1))
                last.then_inc(s_layer, 1)


def kernel(**inputs):
    import numpy as np
    import concourse.bacc as bacc
    from concourse.bass_utils import run_bass_kernel_spmd

    given = {k: np.asarray(v) for k, v in inputs.items()}
    pair = {}
    for i in range(F):
        for j in range(i + 1, F):
            pair[i, j] = len(pair)

    kernels = given["L0_rec_kernels"]
    kmat = np.zeros((len(TILES), D, 2, D), kernels.dtype)
    w_top1 = given["W_top1"]
    w1 = np.zeros((Z_TILES, PART, H1), w_top1.dtype)
    for t, (i, m) in enumerate(TILES):
        zt, row = z_row(t)
        for r in range(2):
            if 2 * m + r > i:
                p = pair[i, 2 * m + r]
                kmat[t, :, r] = kernels[p]
                w1[zt, row + r] = w_top1[F + p]
    for f in range(F):
        m = f // 2
        w1[-1, ROWS * (m % GROUP) + 2 * (m // GROUP) + f % 2] = w_top1[f]
    w1[-1, DENSE_ROW:DENSE_ROW + DENSE] = w_top1[F + len(pair):]
    kmat = kmat.reshape(K_CHUNKS, TILES_A_CHUNK, D, PART).transpose(0, 2, 1, 3).reshape(K_CHUNKS, D, K_CHUNK)
    arrays = {
        "ids": given["ids"].reshape(HALVES * BT, PART, F).transpose(1, 0, 2).reshape(PART, -1),
        "kmat": kmat,
        "dense_t": given["dense_ctx"].T,
        "w1": w1.transpose(1, 0, 2),
        "b1": given["b_top1"].reshape(-1, PART).T,
        "w2": given["W_top2"].reshape(-1, PART, H2).transpose(1, 0, 2),
        "b2": given["b_top2"].reshape(-1, PART).T,
        "w3": given["W_top3"].reshape(-1, PART).T,
        **{f"tbl_{f}": given[f"tbl_{f}"] for f in range(F)},
    }
    arrays = {f"in_{k}": np.ascontiguousarray(v) for k, v in arrays.items()}
    nc = bacc.Bacc("TRN2", target_bir_lowering=False, num_devices=1)
    aps = {k[3:]: nc.dram_tensor(k, a.shape, mybir.dt.from_np(a.dtype), kind="ExternalInput").ap()
           for k, a in arrays.items()}
    out = nc.dram_tensor("out_y", (1, B), mybir.dt.float32, kind="ExternalOutput").ap()
    tables = [aps.pop(f"tbl_{f}") for f in range(F)]
    build(nc, tables=tables, out=out, **aps)
    result = run_bass_kernel_spmd(nc, [arrays], core_ids=[0])
    return result.results[0]["out_y"].reshape(B, 1)
```

```python
import concourse.bass as bass
from concourse import mybir
from contextlib import ExitStack

PART = 128
B = 1024
F = 32
D = 64
NF = F // 2
DENSE = 16
H1, H2 = 512, 256
HB = 512
HALVES = B // HB
BT = HB // PART
GROUP = 4
ROWS = 32
PER_Z = GROUP * (ROWS // 2)
DENSE_ROW = 8


def tile_order():
    order = []
    for i in range(F - 2, -1, -1):
        ms = list(range((i + 1) // 2, NF))
        order += [(i, m) for m in (ms if i % 2 else ms[::-1])]
    return order


TILES = tile_order()
UNITS = len(TILES) // 2
for _u in range(UNITS):
    if TILES[2 * _u][1] > TILES[2 * _u + 1][1]:
        TILES[2 * _u], TILES[2 * _u + 1] = TILES[2 * _u + 1], TILES[2 * _u]
Z_TILES = len(TILES) // PER_Z + 1
K_COLS = len(TILES) * PART
K_CHUNK = 1024
K_HALF = K_CHUNK // 2
K_CHUNKS = K_COLS // K_CHUNK
TILES_A_CHUNK = K_CHUNK // PART


def z_row(t):
    g = t // GROUP
    return t // PER_Z, ROWS * (t % GROUP) + 2 * (g % (ROWS // 2))


def build(nc, ids, tables, kmat, dense_t, w1, b1, w2, b2, w3, out):
    fp32, fp32r, i32 = mybir.dt.float32, mybir.dt.float32r, mybir.dt.int32
    ALU = mybir.AluOpType

    T_SLOTS = 3
    P_SLOTS = 4
    X_SLOTS = 4
    XA_SLOTS = 4
    K_SLOTS = 3
    PAIR_ROWS = 2 * D
    K_AHEAD = 4
    N1, N2 = H1 // PART, H2 // PART

    z_dram = nc.dram_tensor("z_scratch", (Z_TILES, PART, B), fp32, kind="Internal").ap()

    with ExitStack() as ctx:
        def sb(name, shape, dt=fp32):
            return ctx.enter_context(nc.sbuf_tensor(name, shape, dt))

        def sem(name):
            return ctx.enter_context(nc.semaphore(name))

        k_split = sb("k_split", [PART, K_COLS], fp32r)
        x2 = sb("x2", [PART, NF, HB])
        k_raw = sb("k_raw", [PART, K_SLOTS, K_HALF])
        prod = sb("prod", [PART, P_SLOTS, 2 * HB])
        x_high = sb("x_high", [PART, XA_SLOTS, HB], fp32r)
        x_low = sb("x_low", [PART, XA_SLOTS, HB], fp32r)
        x_nat = sb("x_nat", [PART, X_SLOTS, BT, PAIR_ROWS])
        z_out = sb("z_out", [PART, HB])
        ids_all = sb("ids_all", [PART, HALVES * BT * F], i32)
        ids_now = sb("ids_now", [PART, BT * F], i32)
        ident = sb("ident", [PART, PART])
        SEL0 = ROWS - 2
        select = sb("select", [PART, SEL0 + ROWS])
        b1_sb = sb("b1_sb", [PART, N1])
        b2_sb = sb("b2_sb", [PART, N2])
        w3_sb = sb("w3_sb", [PART, N2])

        t_ps = ctx.enter_context(nc.psum_tensor("t_ps", [PART, T_SLOTS, 2 * HB], fp32))
        z_ps = ctx.enter_context(nc.psum_tensor("z_ps", [PART, HB], fp32))
        xt_ps = ctx.enter_context(nc.psum_tensor("xt_ps", [PART, HB], fp32))

        h1_sb = prod[:, :, :].rearrange("p s (t b) -> p (s t) b", b=HB)
        h2_sb = x2[:, 0:HALVES * N2, :]
        y_sb = x2[0:1, HALVES * N2:HALVES * N2 + HALVES, :]

        def parts(at, n):
            return k_split[:, at:at + n], k_split[:, at + n:at + 2 * n]

        at_z = 2 * Z_TILES * H1
        at_w2 = at_z + 2 * HALVES * Z_TILES * HB
        at_h1 = at_w2 + 2 * N1 * H2
        w1_parts = [parts(2 * k * H1, H1) for k in range(Z_TILES)]
        z_parts = [[parts(at_z + 2 * (hb * Z_TILES + k) * HB, HB) for k in range(Z_TILES)] for hb in range(HALVES)]
        w2_parts = parts(at_w2, N1 * H2)
        h1_parts = [parts(at_h1 + 2 * q * HB, HB) for q in range(HALVES * N1)]
        assert H1 == HB == K_HALF and N1 * H2 == 2 * K_HALF
        PARTS_FREE = at_h1 // (2 * PART)

        s_small = sem("small_loaded")
        s_kraw = [sem(f"k_raw_loaded{n}") for n in range(K_SLOTS)]
        s_khigh = sem("k_high_ready")
        s_klow = sem("k_low_ready")
        s_ksplit = sem("k_split_ready")
        s_const = sem("constants_ready")
        s_ids = sem("ids_now_ready")
        s_pairs = sem("pool_went_on")
        s_gather = [sem(f"gathered{n}") for n in range(X_SLOTS)]
        s_xt = sem("x_transposed")
        s_x2 = sem("x2_ready")
        s_xhigh = sem("x_high_ready")
        s_xlow = sem("x_low_ready")
        s_xsplit = sem("x_split_ready")
        s_t = sem("t_ready")
        s_prod = sem("prod_ready")
        s_sum = sem("sums_done")
        s_xsum = sem("x_sums_done")
        s_zout = sem("z_out_ready")
        s_zstore = sem("z_stored")
        s_zload = sem("z_loaded")
        s_high = sem("mlp_operands_high")
        s_low = sem("mlp_operands_low")
        s_h1high = sem("h1_high")
        s_h1low = sem("h1_low")
        s_layer = sem("layer_outputs_in_psum")
        s_act = sem("layer_outputs_in_sbuf")
        s_out = sem("out_stored")

        def count(h, per_half, n):
            return h * per_half + (per_half + n)

        GATHERED = 16 * 2 * BT
        ZSTORE_CREDIT = 16

        SUMS = len(TILES) // GROUP
        SUMS_A_Z = PER_Z // GROUP
        SPLITS = F - 1
        LAST_Z = Z_TILES - 1
        units_until = {i: max(n for n, (j, _) in enumerate(TILES) if j == i) // 2 + 1 for i in range(F - 1)}
        first_unit = {i: min(n for n, (j, _) in enumerate(TILES) if j == i) // 2 for i in range(F - 1)}

        XA_SLOT = {i: (F - 2 - i) % XA_SLOTS for i in range(1, F - 1)}
        XA_SLOT[0] = XA_SLOT[3]

        SPLITS_AT, SPLITS_EVERY = PARTS_FREE + 4, 4
        EARLY_AT = [first_unit[0] + n for n in (1, 3, 5)]
        plan = []
        prepared, chunks, across, splits, summed = F, 0, 0, 0, 0

        def prepare_feature():
            nonlocal prepared, chunks, across
            while chunks < min(K_CHUNKS, K_AHEAD + F - prepared):
                while across < chunks - 1:
                    plan.append(("K across", across))
                    across += 1
                plan.append(("K", chunks))
                chunks += 1
            prepared -= 1
            if prepared % 2:
                plan.append(("pair", prepared // 2))
            if prepared < F - 1:
                plan.append(("split", prepared))

        for u in range(UNITS):
            i_now = min(TILES[2 * u][0], TILES[2 * u + 1][0])
            while prepared > (i_now if u > 0 else F - XA_SLOTS):
                prepare_feature()
            while across < chunks and 2 * u + 1 >= across * TILES_A_CHUNK:
                plan.append(("K across", across))
                across += 1
            plan.append(("unit", u))
            while across < chunks:
                plan.append(("K across", across))
                across += 1
            while prepared > max(0 if i_now < 3 else 1, i_now - (XA_SLOTS - 1)):
                prepare_feature()
            if u % 2 == 1 and u >= 3:
                plan.append(("sum", summed))
                summed += 1
            if u == first_unit[0]:
                plan.append(("embedding sums", 0))
            if u >= SPLITS_AT and (u - SPLITS_AT) % SPLITS_EVERY == 0 and splits < 2 * Z_TILES + 2:
                plan.append(("mlp split", splits))
                splits += 1
            if u in EARLY_AT:
                plan.append(("early", EARLY_AT.index(u)))
            if u - 1 in EARLY_AT:
                plan.append(("early low", EARLY_AT.index(u - 1)))
        while summed < SUMS:
            plan.append(("sum", summed))
            summed += 1
        head = plan[:plan.index(("unit", 0))]
        plan = plan[len(head):]
        early = [[("pair", NF - 1), ("split", F - 2)], [("pair", NF - 2), ("split", F - 3)], [("split", F - 4)]]
        assert [x for x in head if x[0] in ("pair", "split")] == sum(early, [])
        z_order = []
        for what, n in plan:
            if what == "sum" and n % SUMS_A_Z == SUMS_A_Z - 1:
                z_order.append(n // SUMS_A_Z)
            elif what == "embedding sums":
                z_order.append(LAST_Z)

        z_slot = {zt: NF - 1 - n for n, zt in enumerate(z_order[:-1])}

        def k_columns(c):
            at = c * K_CHUNK
            return slice(at, at + K_HALF), slice(at + K_HALF, at + K_CHUNK)

        def own_rows(i):
            return (slice(0, D), slice(D, PART)) if i % 2 == 0 else (slice(D, PART), slice(0, D))

        def x2_free(m):
            return max(u for u in range(UNITS) if m in (TILES[2 * u][1], TILES[2 * u + 1][1])) + 1

        SPLIT = [x for zt in z_order for x in (("w1", 0, zt), ("z", 0, zt))] + [("w2", 0, 0), ("w2", 0, 1)]
        STAGED = len(SPLIT)
        SPLIT += [("z", 1, zt) for zt in z_order]

        def staged_count(n):
            slot = n % K_SLOTS
            items = [SPLIT[k] for k in range(slot, n + 1, K_SLOTS)]
            return 16 * len(range(slot, K_CHUNKS, K_SLOTS)) + sum(48 if x == ("z", 0, LAST_Z) else 16 for x in items)

        def split_operands(n):
            kind, hb, k = SPLIT[n]
            if n < STAGED:
                source = k_raw[:, n % K_SLOTS, :]
            else:
                source = x2[:, z_slot[k], :] if k in z_slot else z_out[:, :]
            if kind == "w2":
                return source, [part[:, k * K_HALF:k * K_HALF + K_HALF] for part in w2_parts]
            return source, (w1_parts[k] if kind == "w1" else z_parts[hb][k])

        LAYERS = [(1, hb, n) for hb in range(HALVES) for n in range(N1)]
        LAYERS += [(2, hb, n) for hb in range(HALVES) for n in range(N2)]
        LAYERS += [(3, hb, 0) for hb in range(HALVES)]
        BANKS = 2 * T_SLOTS + 2

        def bank(q):
            q = q % BANKS
            return t_ps[:, q // 2, q % 2 * HB:q % 2 * HB + HB] if q < 2 * T_SLOTS else (z_ps, xt_ps)[q % 2][:, :]

        block = ctx.enter_context(nc.Block())

        @block.sync
        def _(sp):
            sp.dma_start(ids_all[:, :], ids).then_inc(s_small, 16)
            sp.dma_start(b1_sb[:, :], b1).then_inc(s_small, 16)
            sp.dma_start(b2_sb[:, :], b2).then_inc(s_small, 16)
            sp.dma_start(w3_sb[:, :], w3).then_inc(s_zstore, 16)

            def load_k(chunk, slot):
                sp.dma_start(k_raw[:, slot, :], chunk).then_inc(s_kraw[slot], 16)

            for slot in range(K_SLOTS):
                load_k(kmat[slot], slot)
            rounds, left = K_CHUNKS // K_SLOTS, K_CHUNKS % K_SLOTS
            with sp.Fori(1, rounds) as r:
                for slot in range(K_SLOTS):
                    sp.wait_ge(s_ksplit, r * (2 * K_SLOTS) + 2 * (slot + 1 - K_SLOTS))
                    load_k(kmat[bass.ds(r * K_SLOTS + slot, 1)].rearrange("c p n -> (c p) n"), slot)
            for slot in range(left):
                sp.wait_ge(s_ksplit, 2 * ((rounds - 1) * K_SLOTS + slot + 1))
                load_k(kmat[rounds * K_SLOTS + slot], slot)
            def load_z(hb, zt, dst, loaded):
                sp.wait_ge(s_zstore, 16 * (hb * Z_TILES + z_order.index(zt) + 1) + ZSTORE_CREDIT)
                src = z_dram[zt][:, hb * HB:hb * HB + HB]
                if zt < LAST_Z:
                    sp.dma_start(dst, src).then_inc(loaded, 16)
                else:
                    lo, hi = DENSE_ROW, DENSE_ROW + DENSE
                    sp.dma_start(dst[0:lo], src[0:lo, :]).then_inc(loaded, 16)
                    sp.dma_start(dst[lo:hi], dense_t[:, hb * HB:hb * HB + HB]).then_inc(loaded, 16)
                    sp.dma_start(dst[hi:PART], src[hi:PART, :]).then_inc(loaded, 16)

            sp.wait_ge(s_ksplit, 2 * K_CHUNKS)
            for n, (kind, hb, k) in enumerate(SPLIT[:STAGED]):
                slot = n % K_SLOTS
                if n >= K_SLOTS:
                    sp.wait_ge(s_low, n - K_SLOTS + 1)
                if kind == "z":
                    load_z(hb, k, k_raw[:, slot, :], s_kraw[slot])
                else:
                    src = w1[:, k] if kind == "w1" else w2[:, k]
                    sp.dma_start(k_raw[:, slot, :], src).then_inc(s_kraw[slot], 16)
            sp.wait_ge(s_xsum, count(HALVES, 1, 0))
            for zt in z_order[:-1]:
                sp.wait_ge(s_prod, count(HALVES - 1, UNITS, x2_free(z_slot[zt])))
                load_z(1, zt, x2[:, z_slot[zt], :], s_zload)
            sp.wait_ge(s_act, len(LAYERS))
            sp.dma_start(out, y_sb).then_inc(s_out, 16)
            sp.wait_ge(s_out, 16)

        @block.gpsimd
        def _(pool):
            nc.gpsimd.memset(ident[:, :], 0.0).then_inc(s_const, 1)
            nc.gpsimd.memset(select[:, :], 0.0).then_inc(s_const, 1)
            pool.wait_ge(s_const, 2)
            nc.gpsimd.affine_select(out=ident[:, :], in_=ident[:, :], compare_op=ALU.not_equal, fill=1.0,
                                    base=0, pattern=[[-1, PART]], channel_multiplier=1).then_inc(s_const, 1)
            pool.wait_ge(s_const, 3)
            nc.gpsimd.memset(select[0:D, SEL0:SEL0 + 1], 1.0).then_inc(s_const, 1)
            pool.wait_ge(s_const, 4)
            nc.gpsimd.memset(select[D:PART, SEL0 + 1:SEL0 + 2], 1.0).then_inc(s_const, 1)
            pool.sem_inc(s_xt, NF)
            pool.sem_inc(s_x2, NF)
            pool.sem_inc(s_t, UNITS)
            pool.sem_inc(s_prod, UNITS)
            pool.sem_inc(s_sum, SUMS)
            pool.sem_inc(s_xsum, 1)
            pool.sem_inc(s_zout, Z_TILES)
            pool.wait_ge(s_const, 5)
            pool.wait_ge(s_small, 48)
            nc.gpsimd.tensor_copy(ids_now[:, :], ids_all[:, 0:BT * F]).then_inc(s_ids, 1)
            with pool.Fori(0, HALVES) as h:
                pool.wait_ge(s_ids, h + 1)
                pool.sem_inc(s_pairs, 1)
                for n in range(NF):
                    m, slot = NF - 1 - n, n % X_SLOTS
                    pool.wait_ge(s_xt, count(h, NF, n + 1 - X_SLOTS))
                    pool.sem_inc(s_pairs, 1)
                    for r in (1, 0):
                        f = 2 * m + r
                        for bt in range(BT):
                            nc.gpsimd.indirect_dma_start(
                                x_nat[:, slot, bt, D * r:D * r + D], None, tables[f],
                                bass.IndirectOffsetOnAxis(ap=ids_now[:, bt * F + f:bt * F + f + 1], axis=0),
                            ).then_inc(s_gather[slot], 16)
                for slot in range(X_SLOTS):
                    pool.wait_ge(s_gather[slot], (h + 1) * (GATHERED * NF // X_SLOTS))
                    pool.sem_inc(s_pairs, 1)
                nc.gpsimd.tensor_copy(ids_now[:, :], ids_all[:, bass.ds((HALVES - 1 - h) * (BT * F), BT * F)])\
                    .then_inc(s_ids, 1)

        @block.scalar
        def _(act):
            def pair(h, m):
                act.wait_ge(s_xt, count(h, NF, NF - m))
                act.wait_ge(s_prod, count(h, UNITS, x2_free(m) - UNITS))
                if m == NF - 1:
                    act.wait_ge(s_xsum, count(h, 1, 0))
                nc.scalar.copy(x2[:, m, :], xt_ps[:, :]).then_inc(s_x2, 1)

            def high_part(h, i):
                own, other = own_rows(i)
                act.wait_ge(s_x2, count(h, NF, NF - i // 2))
                before = min((j for j in range(i + 1, F - 1) if XA_SLOT[j] == XA_SLOT[i]), default=None)
                if before is not None:
                    act.wait_ge(s_t, count(h, UNITS, units_until[before]))
                else:
                    last = min(j for j in range(F - 1) if XA_SLOT[j] == XA_SLOT[i])
                    act.wait_ge(s_t, count(h, UNITS, units_until[last] - UNITS))
                nc.scalar.copy(x_high[own, XA_SLOT[i], :], x2[own, i // 2, :]).then_inc(s_xhigh, 1)
                nc.scalar.copy(x_high[other, XA_SLOT[i], :], x2[own, i // 2, :])

            def low_part_across(h, i):
                own, other = own_rows(i)
                act.wait_ge(s_xlow, h * SPLITS + (F - 1 - i))
                nc.scalar.copy(x_low[other, XA_SLOT[i], :], x_low[own, XA_SLOT[i], :]).then_inc(s_xsplit, 1)

            def k_high(c):
                first, _ = k_columns(c)
                act.wait_ge(s_kraw[c % K_SLOTS], 16 * (c // K_SLOTS + 1))
                nc.scalar.copy(k_split[:, first], k_raw[:, c % K_SLOTS, :]).then_inc(s_khigh, 1)

            def k_across(c):
                first, second = k_columns(c)
                act.wait_ge(s_klow, c + 1)
                nc.scalar.copy(k_split[D:PART, first], k_split[0:D, second]).then_inc(s_ksplit, 1)
                act.wait_ge(s_ksplit, 2 * c + 1)
                nc.scalar.copy(k_split[0:D, second], k_raw[D:PART, c % K_SLOTS, :]).then_inc(s_ksplit, 1)

            def mlp_high(n):
                if n == 0:
                    act.wait_ge(s_t, count(HALVES - 1, UNITS, PARTS_FREE))
                if n < STAGED:
                    act.wait_ge(s_kraw[n % K_SLOTS], staged_count(n))
                elif n == STAGED:
                    act.wait_ge(s_zload, 16 * (Z_TILES - 1 + 2))
                elif n == len(SPLIT) - 1:
                    act.wait_ge(s_zout, count(HALVES, Z_TILES, 0))
                source, (high, _) = split_operands(n)
                nc.scalar.copy(high, source).then_inc(s_high, 1)

            for what, k in head:
                if what == "K":
                    k_high(k)
                elif what == "K across":
                    k_across(k)
                elif what == "pair":
                    pair(0, k)
                else:
                    high_part(0, k)
                    low_part_across(0, k)

            with act.Fori(0, HALVES) as h:
                def z_tile(n, src):
                    act.wait_ge(s_zstore, h * (16 * Z_TILES) + (16 * n + ZSTORE_CREDIT))
                    nc.scalar.copy(z_out[:, :], src[:, :]).then_inc(s_zout, 1)
                    act.wait_ge(s_zout, count(h, Z_TILES, n + 1))
                    act.dma_start(z_dram[z_order[n]][:, bass.ds(h * HB, HB)], z_out[:, :]).then_inc(s_zstore, 16)

                n = 0
                waiting = []
                for what, k in plan:
                    if waiting and (what in ("split", "sum") or what == "unit" and k >= first_unit[waiting[0]]):
                        low_part_across(h, waiting.pop(0))
                    if what in ("K", "K across"):
                        with act.If(h < 1):
                            k_high(k) if what == "K" else k_across(k)
                    elif what == "pair":
                        pair(h, k)
                    elif what == "split":
                        high_part(h, k)
                        waiting.append(k)
                    elif what == "mlp split":
                        with act.If(h > HALVES - 2):
                            mlp_high(k)
                    elif what == "early":
                        with act.If(h < HALVES - 1):
                            for step, x in early[k]:
                                pair(h + 1, x) if step == "pair" else high_part(h + 1, x)
                    elif what == "early low":
                        with act.If(h < HALVES - 1):
                            low_part_across(h + 1, early[k][-1][1])
                    elif what == "sum" and k % SUMS_A_Z == SUMS_A_Z - 1:
                        act.wait_ge(s_sum, count(h, SUMS, k + 1))
                        z_tile(n, z_ps)
                        n += 1
                    elif what == "embedding sums":
                        act.wait_ge(s_xsum, count(h, 1, 1))
                        z_tile(n, xt_ps)
                        n += 1

            act.wait_ge(s_t, count(HALVES, UNITS, 0))
            for n in range(STAGED, len(SPLIT)):
                mlp_high(n)
            for q in range(HALVES * N1):
                act.wait_ge(s_act, q + 1)
                nc.scalar.copy(h1_parts[q][0], h1_sb[:, q, :]).then_inc(s_h1high, 1)
            act.wait_ge(s_zstore, 16 * HALVES * Z_TILES + ZSTORE_CREDIT)

        @block.vector
        def _(dve):
            def low_part(h, i):
                own, _ = own_rows(i)
                dve.wait_ge(s_xhigh, h * SPLITS + (F - 1 - i))
                nc.vector.tensor_tensor(x_low[own, XA_SLOT[i], :], x2[own, i // 2, :],
                                        x_high[own, XA_SLOT[i], :].bitcast(fp32), ALU.subtract).then_inc(s_xlow, 1)

            def k_low(c):
                first, second = k_columns(c)
                dve.wait_ge(s_khigh, c + 1)
                nc.vector.tensor_tensor(k_split[:, second], k_raw[:, c % K_SLOTS, :],
                                        k_split[:, first].bitcast(fp32), ALU.subtract).then_inc(s_klow, 1)

            def mlp_low(n):
                source, (high, low) = split_operands(n)
                dve.wait_ge(s_high, n + 1)
                nc.vector.tensor_tensor(low, source, high.bitcast(fp32), ALU.subtract).then_inc(s_low, 1)

            for what, k in head:
                if what == "K":
                    k_low(k)
                elif what == "split":
                    low_part(0, k)

            with dve.Fori(0, HALVES) as h:
                waiting = []
                for what, k in plan:
                    if what in ("K", "split", "sum") and waiting:
                        low_part(h, waiting.pop(0))
                    if what == "K":
                        with dve.If(h < 1):
                            k_low(k)
                    if what == "split":
                        waiting.append(k)
                    if what == "mlp split":
                        with dve.If(h > HALVES - 2):
                            mlp_low(k)
                    if what == "early low":
                        with dve.If(h < HALVES - 1):
                            low_part(h + 1, early[k][-1][1])
                    if what != "unit":
                        continue
                    (ia, ma), (ib, mb) = TILES[2 * k], TILES[2 * k + 1]
                    if waiting and waiting[0] >= min(ia, ib):
                        low_part(h, waiting.pop(0))
                    dve.wait_ge(s_t, count(h, UNITS, k + 1))
                    if k == first_unit[min(ia, ib)]:
                        dve.wait_ge(s_x2, count(h, NF, NF - min(ia, ib) // 2))
                    if k % 2 == 0:
                        dve.wait_ge(s_sum, count(h, SUMS, k // 2 + 1 - P_SLOTS // 2))
                    if ma == mb:
                        xj = x2[:, ma:ma + 1, :].broadcast_to([PART, 2, HB])
                    else:
                        xj = x2[:, ma:mb + 1, :]
                    view = lambda t: t.rearrange("p (t b) -> p t b", b=HB)
                    nc.vector.tensor_tensor(view(prod[:, k % P_SLOTS, :]), view(t_ps[:, k % T_SLOTS, :]), xj,
                                            ALU.mult).then_inc(s_prod, 1)
                    if waiting:
                        low_part(h, waiting.pop(0))

            for n in range(STAGED, len(SPLIT)):
                mlp_low(n)
            def h1_low_part(q):
                high, low = h1_parts[q]
                dve.wait_ge(s_h1high, q + 1)
                nc.vector.tensor_tensor(low, h1_sb[:, q, :], high.bitcast(fp32), ALU.subtract).then_inc(s_h1low, 1)

            dve.wait_ge(s_small, 48)
            dve.wait_ge(s_sum, count(HALVES, SUMS, 0))
            dve.wait_ge(s_prod, count(HALVES, UNITS, 0))
            for q, (layer, hb, n) in enumerate(LAYERS):
                dve.wait_ge(s_layer, q + 1)
                if layer == 3:
                    nc.vector.tensor_copy(y_sb[0:1, hb, :], bank(q)[0:1, :]).then_inc(s_act, 1)
                else:
                    bias, dst = (b1_sb, h1_sb[:, q, :]) if layer == 1 else (b2_sb, h2_sb[:, hb * N2 + n, :])
                    nc.vector.tensor_scalar(dst, bank(q), bias[:, n:n + 1], 0.0, ALU.add, ALU.max).then_inc(s_act, 1)
                if 1 <= q <= HALVES * N1:
                    h1_low_part(q - 1)

        @block.tensor
        def _(pe):
            pe.wait_ge(s_const, 5)
            def pair(h, m):
                n, slot = NF - 1 - m, (NF - 1 - m) % X_SLOTS
                pe.wait_ge(s_gather[slot], h * (GATHERED * NF // X_SLOTS) + GATHERED * (n // X_SLOTS + 1))
                if n == 0:
                    pe.wait_ge(s_zout, count(h, Z_TILES, z_order.index(LAST_Z) + 1 - Z_TILES))
                pe.wait_ge(s_x2, count(h, NF, n))
                for bt in range(BT):
                    last = nc.tensor.transpose(xt_ps[:, bt * PART:bt * PART + PART], x_nat[:, slot, bt, :], ident[:, :])
                last.then_inc(s_xt, 1)

            for what, k in head:
                if what == "pair":
                    pair(0, k)

            with pe.Fori(0, HALVES) as h:
                def unit(u):
                    pe.wait_ge(s_prod, count(h, UNITS, max(u + 1 - T_SLOTS, 0)))
                    for t in (2 * u, 2 * u + 1):
                        i, m = TILES[t]
                        if u == first_unit[i]:
                            pe.wait_ge(s_xsplit, h * SPLITS + (F - 1 - i))
                        if t % TILES_A_CHUNK == 0:
                            pe.wait_ge(s_ksplit, 2 * (t // TILES_A_CHUNK + 1))
                        dst = t_ps[:, u % T_SLOTS, t % 2 * HB:t % 2 * HB + HB]
                        weights = k_split[:, t * PART:t * PART + PART]
                        nc.tensor.matmul(dst, weights, x_high[:, XA_SLOT[i], :], start=True, stop=False)
                        last = nc.tensor.matmul(dst, weights, x_low[:, XA_SLOT[i], :], start=False, stop=True)
                    last.then_inc(s_t, 1)

                def selector(k):
                    return select[:, SEL0 - 2 * k:SEL0 - 2 * k + ROWS]

                def sum_round(g):
                    pe.wait_ge(s_prod, count(h, UNITS, 2 * g + 2))
                    k = g % SUMS_A_Z
                    if g == 0:
                        pe.wait_ge(s_zout, count(h, Z_TILES, 0))
                    elif k == 0:
                        pe.wait_ge(s_zout, count(h, Z_TILES, z_order.index(g // SUMS_A_Z - 1) + 1))
                    for c in range(GROUP):
                        u = 2 * g + c // 2
                        last = nc.tensor.matmul(z_ps[ROWS * c:ROWS * c + ROWS, :], selector(k),
                                                prod[:, u % P_SLOTS, c % 2 * HB:c % 2 * HB + HB],
                                                start=(k == 0), stop=(k == SUMS_A_Z - 1))
                    last.then_inc(s_sum, 1)

                def embedding_sums():
                    pe.wait_ge(s_x2, count(h, NF, NF))
                    for m in range(NF):
                        k, c = m // GROUP, m % GROUP
                        last = nc.tensor.matmul(xt_ps[ROWS * c:ROWS * c + ROWS, :], selector(k), x2[:, m, :],
                                                start=(k == 0), stop=(k == NF // GROUP - 1))
                    last.then_inc(s_xsum, 1)

                for what, k in plan:
                    if what == "pair":
                        pair(h, k)
                    elif what == "unit":
                        unit(k)
                    elif what == "sum":
                        sum_round(k)
                    elif what == "embedding sums":
                        embedding_sums()
                    elif what == "early":
                        if early[k][0][0] == "pair":
                            with pe.If(h < HALVES - 1):
                                pair(h + 1, early[k][0][1])

            def product(dst, w, x, cols, first, last_one):
                (wh, wl), (xh, xl) = w, x
                nc.tensor.matmul(dst, wh[:, cols], xh, start=first, stop=False)
                nc.tensor.matmul(dst, wl[:, cols], xh, start=False, stop=False)
                return nc.tensor.matmul(dst, wh[:, cols], xl, start=False, stop=last_one)

            pe.wait_ge(s_prod, count(HALVES, UNITS, 0))
            for hb in range(HALVES):
                if hb > 0:
                    pe.wait_ge(s_zout, count(HALVES, Z_TILES, 0))
                for k in z_order:
                    pe.wait_ge(s_low, SPLIT.index(("z", hb, k)) + 1)
                    for n in range(N1):
                        last = product(bank(hb * N1 + n), w1_parts[k], z_parts[hb][k],
                                       slice(n * PART, n * PART + PART), k == z_order[0], k == z_order[-1])
                        if k == z_order[-1]:
                            last.then_inc(s_layer, 1)
            for hb in range(HALVES):
                for n in range(N2):
                    q = LAYERS.index((2, hb, n))
                    pe.wait_ge(s_act, q - BANKS + 1)
                    for k in range(N1):
                        pe.wait_ge(s_h1low, hb * N1 + k + 1)
                        last = product(bank(q), w2_parts, h1_parts[hb * N1 + k],
                                       slice(k * H2 + n * PART, k * H2 + n * PART + PART), k == 0, k == N1 - 1)
                    last.then_inc(s_layer, 1)
            for hb in range(HALVES):
                q = LAYERS.index((3, hb, 0))
                pe.wait_ge(s_act, LAYERS.index((2, hb, N2 - 1)) + 1)
                for k in range(N2):
                    last = nc.tensor.matmul(bank(q)[0:1, :], w3_sb[:, k:k + 1], h2_sb[:, hb * N2 + k, :],
                                            start=(k == 0), stop=(k == N2 - 1))
                last.then_inc(s_layer, 1)


def kernel(**inputs):
    import numpy as np
    import concourse.bacc as bacc
    from concourse.bass_utils import run_bass_kernel_spmd

    given = {k: np.asarray(v) for k, v in inputs.items()}
    pair = {}
    for i in range(F):
        for j in range(i + 1, F):
            pair[i, j] = len(pair)

    kernels = given["L0_rec_kernels"]
    kmat = np.zeros((len(TILES), D, 2, D), kernels.dtype)
    w_top1 = given["W_top1"]
    w1 = np.zeros((Z_TILES, PART, H1), w_top1.dtype)
    for t, (i, m) in enumerate(TILES):
        zt, row = z_row(t)
        for r in range(2):
            if 2 * m + r > i:
                p = pair[i, 2 * m + r]
                kmat[t, :, r] = kernels[p]
                w1[zt, row + r] = w_top1[F + p]
    for f in range(F):
        m = f // 2
        w1[-1, ROWS * (m % GROUP) + 2 * (m // GROUP) + f % 2] = w_top1[f]
    w1[-1, DENSE_ROW:DENSE_ROW + DENSE] = w_top1[F + len(pair):]
    kmat = kmat.reshape(K_CHUNKS, 2, TILES_A_CHUNK // 2, D, PART).transpose(0, 1, 3, 2, 4).reshape(K_CHUNKS, PART, K_HALF)
    arrays = {
        "ids": given["ids"].reshape(HALVES * BT, PART, F).transpose(1, 0, 2).reshape(PART, -1),
        "kmat": kmat,
        "dense_t": given["dense_ctx"].T,
        "w1": w1.transpose(1, 0, 2),
        "b1": given["b_top1"].reshape(-1, PART).T,
        "w2": given["W_top2"].reshape(-1, PART, H2).transpose(1, 0, 2).reshape(PART, 2, -1),
        "b2": given["b_top2"].reshape(-1, PART).T,
        "w3": given["W_top3"].reshape(-1, PART).T,
        **{f"tbl_{f}": given[f"tbl_{f}"] for f in range(F)},
    }
    arrays = {f"in_{k}": np.ascontiguousarray(v) for k, v in arrays.items()}
    nc = bacc.Bacc("TRN2", target_bir_lowering=False, num_devices=1, dynamic_dma_scratch_size=4096)
    aps = {k[3:]: nc.dram_tensor(k, a.shape, mybir.dt.from_np(a.dtype), kind="ExternalInput").ap()
           for k, a in arrays.items()}
    out = nc.dram_tensor("out_y", (1, B), mybir.dt.float32, kind="ExternalOutput").ap()
    tables = [aps.pop(f"tbl_{f}") for f in range(F)]
    build(nc, tables=tables, out=out, **aps)
    result = run_bass_kernel_spmd(nc, [arrays], core_ids=[0])
    return result.results[0]["out_y"].reshape(B, 1)
```
